# Optimizing a Trainium2 kernel written in Bass

```python
import numpy as np
import jax
import jax.numpy as jnp

def _softmax(x, axis=-1):
    return jax.nn.softmax(x, axis=axis)
def _gelu(x):
    return jax.nn.gelu(x, approximate=True)
def _silu(x):
    return jax.nn.silu(x)
def _sigmoid(x):
    return jax.nn.sigmoid(x)
def _layernorm(x, axis=-1, eps=1e-5):
    m = jnp.mean(x, axis=axis, keepdims=True)
    v = jnp.var(x, axis=axis, keepdims=True)
    return (x - m) / jnp.sqrt(v + eps)
def _scatter_add(tgt, idx, src, axis=0):
    return tgt.at[idx].add(src)
def _segment_sum(src, seg, n):
    return jax.ops.segment_sum(src, seg, n)

kernel_name = 'mk_rec_standalone_d1_rec_55a00e'

def setup_inputs(seed: int = 0):
    np.random.seed(seed)
    _w = jnp.asarray
    def _rec_inputs():
        import jax
        import jax.numpy as jnp
        _rk = jax.random.key(seed)
        r_emb_inputs = 7.22013e-05 + 1.00017 * jax.random.normal(jax.random.fold_in(_rk, 1), (4096, 16, 256), jnp.float32)
        return r_emb_inputs
    r_emb_inputs = _rec_inputs()
    def _L0_rec_setup():
        import jax, jax.numpy as jnp
        import numpy as np
        NUM_FIELDS = 16
        EMBED = 256
        BATCH = 2048
        NUM_PAIRS = NUM_FIELDS * (NUM_FIELDS - 1) // 2
        key = jax.random.key(seed)
        k1, k2, k3 = jax.random.split(key, 3)
        emb_inputs = jax.random.normal(k1, (BATCH, NUM_FIELDS, EMBED), dtype=jnp.float32)
        bound = 1.0 / np.sqrt(NUM_PAIRS)
        weight = jax.random.uniform(k2, (NUM_PAIRS, EMBED, EMBED), dtype=jnp.float32, minval=-bound, maxval=bound)
        bias = jax.random.uniform(k3, (NUM_PAIRS, EMBED), dtype=jnp.float32, minval=-bound, maxval=bound)
        return {'emb_inputs': emb_inputs, 'weight': weight, 'bias': bias}
    _L0_rec_all = _L0_rec_setup()
    _L0_rec_in = {k: v for k, v in _L0_rec_all.items() if k in ('weight', 'bias', )}
    del _L0_rec_all

    return {
        "r_emb_inputs": r_emb_inputs,
        "L0_rec_weight": _L0_rec_in["weight"],
        "L0_rec_bias": _L0_rec_in["bias"],
    }

def reference(r_emb_inputs, L0_rec_weight, L0_rec_bias):
    import jax
    import jax.numpy as jnp
    def _L0_rec_ref(emb_inputs, weight, bias):
        import jax, jax.numpy as jnp
        import numpy as np
        NUM_FIELDS = 16
        EMBED = 256
        BATCH = 2048
        NUM_PAIRS = NUM_FIELDS * (NUM_FIELDS - 1) // 2
        row_idx, col_idx = np.triu_indices(NUM_FIELDS, k=1)
        p = emb_inputs[:, row_idx]
        q = emb_inputs[:, col_idx]
        out = jnp.einsum('bpe,pef->bpf', p, weight) * q + bias
        return out

    y = _L0_rec_ref(r_emb_inputs, L0_rec_weight, L0_rec_bias)
    return y


_drawn_inputs = setup_inputs


def setup_inputs(seed=0):
    import zlib

    import numpy as np

    out = dict(_drawn_inputs(seed))
    spreads = {}
    factors = {}
    for name, (base, spread) in spreads.items():
        noise = np.random.default_rng([zlib.crc32(name.encode()), seed]).standard_normal(out[name].shape)
        drawn = base * np.exp(spread * noise) if base else spread * noise
        out[name] = jnp.asarray(drawn.astype(out[name].dtype))
    for name, factor in factors.items():
        out[name] = (out[name] * factor).astype(out[name].dtype)
    return out
```

```python
from contextlib import ExitStack

import concourse.bass as bass
from concourse import mybir
from concourse.alu_op_type import AluOpType as ALU

F32 = mybir.dt.float32
F32R = mybir.dt.float32r
ACT_IDENTITY = mybir.ActivationFunctionType.Identity

P = 128
BATCH, FIELDS, EMBED = 4096, 16, 256
HALVES = EMBED // P
PAIRS = [(i, j) for i in range(FIELDS) for j in range(i + 1, FIELDS)]
CHUNK = 512
CHUNKS = BATCH // CHUNK

GROUP_FIELDS = 8
PSUM_SLOTS = 4
OUT_SLOTS = 4
PRODUCT_SLOTS = 2
SPLIT_SLOTS = 3
STAGE_SLOTS = 4
LOOKAHEAD = 3
LEAD = 3


class Group:

    def __init__(self, fields, square):
        self.fields = fields
        if square:
            self.rows = GROUP_FIELDS // 2
            self.pairs = [(r, s) for r in range(self.rows) for s in range(self.rows, GROUP_FIELDS)]
            self.split_slot = [0, 1, 0, 1]
        else:
            self.rows = GROUP_FIELDS - 1
            self.pairs = [(r, s) for r in range(self.rows) for s in range(r + 1, GROUP_FIELDS)]
            self.split_slot = [0, 1, 0, 1, 0, 1, 2]
        self.n = len(self.pairs)
        self.first = [min(n for n, (r, _) in enumerate(self.pairs) if r == row) for row in range(self.rows)]
        self.split_at = [[] for _ in self.pairs]
        if square:
            for r in range(self.rows):
                self.split_at[self.first[r]].append(((r + 1) % self.rows, r + 1 == self.rows))
        else:
            for r in range(5):
                self.split_at[self.first[r]].append((r + 1, False))
            self.split_at[self.first[5]] += [(6, False), (0, True)]
        self.load_after = [[] for _ in self.pairs]
        for s in range(GROUP_FIELDS):
            last_use = max([n for n, (_, t) in enumerate(self.pairs) if t == s], default=0)
            if s < self.rows:
                last_use = max(last_use, self.first[s])
            self.load_after[last_use].append(s)


BLOCK = FIELDS // 4
A, B, C, D = ([*range(BLOCK * k, BLOCK * (k + 1))] for k in range(4))
GROUPS = [Group(A + B, False), Group(A + C, True), Group(A + D, True),
          Group(B + C, True), Group(B + D, True), Group(C + D, False)]
WEIGHT_SLOTS = max(g.n for g in GROUPS)
assert sum(g.n for g in GROUPS) == len(PAIRS)
assert all(g.n % PSUM_SLOTS == g.n % OUT_SLOTS == g.n % PRODUCT_SLOTS == 0 for g in GROUPS)

PAIR_BASE = [CHUNKS * sum(g.n for g in GROUPS[:k]) for k in range(len(GROUPS))]
ROW_BASE = [CHUNKS * sum(g.rows for g in GROUPS[:k]) for k in range(len(GROUPS))]

DELAY = 2


def weight_plan():
    plan = [[[n + LOOKAHEAD] if n + LOOKAHEAD < GROUPS[0].n else [] for n in range(GROUPS[0].n)]]
    for old, new in zip(GROUPS, GROUPS[1:]):
        at = [[] for _ in range(old.n)]
        for w in range(min(old.n, new.n)):
            at[min(w + DELAY, old.n - 1)].append(w)
        for w in range(old.n, new.n):
            at[old.n - new.n + w - 1].append(w)
        plan.append(at)
    return plan


WEIGHT_PLAN = weight_plan()
WEIGHT_ORDER = [list(range(LOOKAHEAD)) + [w for at in WEIGHT_PLAN[0] for w in at]]
WEIGHT_ORDER += [[w for at in plan for w in at] for plan in WEIGHT_PLAN[1:]]
WEIGHT_BASE = [sum(g.n for g in GROUPS[:k]) for k in range(len(GROUPS))]
GROUP_PAIRS = [[(g.fields[r], g.fields[s]) for r, s in g.pairs] for g in GROUPS]


def weight_count(g, w):
    return WEIGHT_BASE[g] + WEIGHT_ORDER[g].index(w)


def bilinear_interactions(nc, x, weight, bias, out):
    with ExitStack() as ctx:
        def sb(name, shape, dt):
            return ctx.enter_context(nc.sbuf_tensor(name, shape, dt))

        def sem(name):
            return ctx.enter_context(nc.semaphore(name))

        w_hi = sb("w_hi", [P, WEIGHT_SLOTS, HALVES, EMBED], F32R)
        w_lo = sb("w_lo", [P, WEIGHT_SLOTS, HALVES, EMBED], F32R)
        w_raw = sb("w_raw", [P, STAGE_SLOTS, HALVES, EMBED], F32)
        x_raw = sb("x_raw", [P, GROUP_FIELDS, HALVES, CHUNK], F32)
        x_hi = sb("x_hi", [P, SPLIT_SLOTS, HALVES, CHUNK], F32R)
        x_lo = sb("x_lo", [P, SPLIT_SLOTS, HALVES, CHUNK], F32R)
        product = sb("product", [P, PRODUCT_SLOTS, HALVES, CHUNK], F32)
        result = sb("result", [P, OUT_SLOTS, HALVES, CHUNK], F32)
        bias_sb = sb("bias_sb", [P, len(PAIRS), HALVES], F32)
        xw = ctx.enter_context(nc.psum_tensor("xw", [P, PSUM_SLOTS, HALVES, CHUNK], F32))

        x_loaded = [sem(f"x_loaded{s}") for s in range(GROUP_FIELDS)]
        w_loaded = [sem(f"w_loaded{s}") for s in range(STAGE_SLOTS)]
        bias_loaded = sem("bias_loaded")
        x_hi_made = sem("x_hi_made")
        w_hi_made = sem("w_hi_made")
        x_split = sem("x_split")
        w_split = sem("w_split")
        pair_summed = sem("pair_summed")
        pair_multiplied = sem("pair_multiplied")
        pair_biased = sem("pair_biased")
        stored = [sem(f"stored{s}") for s in range(OUT_SLOTS)]

        block = ctx.enter_context(nc.Block())

        def for_chunks(eng, g, body, last_differs=False):
            begin, end = (1 if g == 0 else 0), CHUNKS - (1 if last_differs else 0)
            if g == 0:
                body(0, True, False)
            with eng.Fori(begin, end) as c:
                body(c, False, False)
            if last_differs:
                body(CHUNKS - 1, False, True)

        def weight_phase(g, first, last):
            if first:
                return 0, WEIGHT_PLAN[0]
            if last and g + 1 < len(GROUPS):
                return g + 1, WEIGHT_PLAN[g + 1]
            return g, [[]] * GROUPS[g].n

        @block.sync
        def _(sp):
            def load_weight(g, w):
                m = weight_count(g, w)
                if m >= STAGE_SLOTS:
                    sp.wait_ge(w_split, m - STAGE_SLOTS + 1)
                sp.dma_start(w_raw[:, m % STAGE_SLOTS], weight[WEIGHT_BASE[g] + w]).then_inc(
                    w_loaded[m % STAGE_SLOTS], 16)

            def load_field(g, slot, c):
                sp.dma_start(x_raw[:, slot], x[GROUPS[g].fields[slot], c]).then_inc(x_loaded[slot], 16)

            load_field(0, 0, 0)
            load_weight(0, 0)
            load_field(0, 1, 0)
            sp.dma_start(bias_sb[:], bias).then_inc(bias_loaded, 16)
            for k in range(2, GROUP_FIELDS):
                if k - 1 < LOOKAHEAD + LEAD:
                    load_weight(0, k - 1)
                load_field(0, k, 0)

            for g, group in enumerate(GROUPS):
                def chunk(c, first, last):
                    new, arriving = weight_phase(g, first, last)
                    if not first:
                        for w in [w for at in arriving[:LEAD] for w in at]:
                            load_weight(new, w)
                    for n in range(group.n):
                        if n + LEAD < group.n:
                            for w in arriving[n + LEAD]:
                                load_weight(new, w)
                        sp.wait_ge(pair_biased, c * group.n + (PAIR_BASE[g] + n + 1))
                        sp.dma_start(out[WEIGHT_BASE[g] + n, c], result[:, n % OUT_SLOTS]).then_inc(
                            stored[n % OUT_SLOTS], 16)
                        for slot in group.load_after[n]:
                            if slot < group.rows:
                                sp.wait_ge(x_split, c * group.rows + (ROW_BASE[g] + slot + 1))
                            if not last:
                                load_field(g, slot, c + 1)
                            elif g + 1 < len(GROUPS):
                                load_field(g + 1, slot, 0)

                for_chunks(sp, g, chunk, last_differs=True)
            for slot in range(OUT_SLOTS):
                sp.wait_ge(stored[slot], 16 * CHUNKS * len(PAIRS) // OUT_SLOTS)

        @block.vector
        def _(dve):
            def make_w_hi(g, w):
                m = weight_count(g, w)
                dve.wait_ge(w_loaded[m % STAGE_SLOTS], 16 * (m // STAGE_SLOTS + 1))
                nc.vector.tensor_copy(w_hi[:, w], w_raw[:, m % STAGE_SLOTS]).then_inc(w_hi_made, 1)

            def make_x_hi(g, row, loads):
                slot = GROUPS[g].split_slot[row]
                dve.wait_ge(x_loaded[row], loads * 16)
                nc.vector.tensor_copy(x_hi[:, slot], x_raw[:, row]).then_inc(x_hi_made, 1)

            make_x_hi(0, 0, 1)
            for w in range(LOOKAHEAD):
                make_w_hi(0, w)

            for g, group in enumerate(GROUPS):
                def chunk(c, first, last):
                    new, arriving = weight_phase(g, first, last)
                    for n, (row, slot) in enumerate(group.pairs):
                        for other, next_chunk in group.split_at[n]:
                            if not next_chunk:
                                make_x_hi(g, other, c + (g * CHUNKS + 1))
                            elif not (last and g + 1 == len(GROUPS)):
                                make_x_hi(g, other, c + (g * CHUNKS + 2))
                        dve.wait_ge(pair_summed, c * group.n + (PAIR_BASE[g] + n + 1))
                        if n < GROUP_FIELDS - 1:
                            dve.wait_ge(x_loaded[slot], c * 16 + 16 * (g * CHUNKS + 1))
                        if not (first and n < PRODUCT_SLOTS):
                            dve.wait_ge(pair_biased, c * group.n + (PAIR_BASE[g] + n + 1 - PRODUCT_SLOTS))
                        nc.vector.tensor_tensor(product[:, n % PRODUCT_SLOTS], xw[:, n % PSUM_SLOTS],
                                                x_raw[:, slot], ALU.mult).then_inc(pair_multiplied, 1)
                        for w in arriving[n]:
                            make_w_hi(new, w)

                for_chunks(dve, g, chunk, last_differs=True)

        @block.gpsimd
        def _(pool):
            def make_w_lo(g, w):
                m = weight_count(g, w)
                pool.wait_ge(w_hi_made, m + 1)
                nc.gpsimd.tensor_tensor(w_lo[:, w], w_raw[:, m % STAGE_SLOTS], w_hi[:, w].bitcast(F32),
                                        ALU.subtract).then_inc(w_split, 1)

            def make_x_lo(g, row, count):
                slot = GROUPS[g].split_slot[row]
                pool.wait_ge(x_hi_made, count)
                nc.gpsimd.tensor_tensor(x_lo[:, slot], x_raw[:, row], x_hi[:, slot].bitcast(F32),
                                        ALU.subtract).then_inc(x_split, 1)

            make_x_lo(0, 0, 1)
            for w in range(LOOKAHEAD):
                make_w_lo(0, w)

            for g, group in enumerate(GROUPS):
                def chunk(c, first, last):
                    new, arriving = weight_phase(g, first, last)
                    for n in range(group.n):
                        for other, next_chunk in group.split_at[n]:
                            if not next_chunk:
                                make_x_lo(g, other, c * group.rows + (ROW_BASE[g] + other + 1))
                            elif not (last and g + 1 == len(GROUPS)):
                                make_x_lo(g, other, c * group.rows + (ROW_BASE[g] + group.rows + other + 1))
                        for w in arriving[n]:
                            make_w_lo(new, w)

                for_chunks(pool, g, chunk, last_differs=True)

        @block.tensor
        def _(pe):
            for g, group in enumerate(GROUPS):
                def chunk(c, first, last):
                    for n, (row, _) in enumerate(group.pairs):
                        if n == group.first[row]:
                            pe.wait_ge(x_split, c * group.rows + (ROW_BASE[g] + row + 1))
                        pe.wait_ge(w_split, weight_count(g, n) + 1)
                        if not (first and n < PSUM_SLOTS):
                            pe.wait_ge(pair_multiplied, c * group.n + (PAIR_BASE[g] + n + 1 - PSUM_SLOTS))
                        s = group.split_slot[row]
                        for half in range(HALVES):
                            f = slice(half * P, (half + 1) * P)
                            for k in range(HALVES):
                                terms = [(w_lo, x_hi), (w_hi, x_lo), (w_hi, x_hi)]
                                for t, (w, xs) in enumerate(terms):
                                    product_done = nc.tensor.matmul(
                                        xw[:, n % PSUM_SLOTS, half], w[:, n, k, f], xs[:, s, k],
                                        start=(k == 0 and t == 0),
                                        stop=(k == HALVES - 1 and t == len(terms) - 1))
                        product_done.then_inc(pair_summed, 1)

                for_chunks(pe, g, chunk)

        @block.scalar
        def _(act):
            act.wait_ge(bias_loaded, 16)
            for g, group in enumerate(GROUPS):
                def chunk(c, first, last):
                    for n in range(group.n):
                        act.wait_ge(pair_multiplied, c * group.n + (PAIR_BASE[g] + n + 1))
                        if not (first and n < OUT_SLOTS):
                            act.wait_ge(stored[n % OUT_SLOTS],
                                        c * (16 * group.n // OUT_SLOTS)
                                        + 16 * ((PAIR_BASE[g] + n) // OUT_SLOTS))
                        for half in range(HALVES):
                            b = WEIGHT_BASE[g] + n
                            added = nc.scalar.activation(result[:, n % OUT_SLOTS, half],
                                                         product[:, n % PRODUCT_SLOTS, half], ACT_IDENTITY,
                                                         bias=bias_sb[:, b, half:half + 1])
                        added.then_inc(pair_biased, 1)

                for_chunks(act, g, chunk)


def kernel(r_emb_inputs, L0_rec_weight, L0_rec_bias):
    import numpy as np
    import concourse.bacc as bacc
    from concourse.bass_utils import run_bass_kernel_spmd

    order = [PAIRS.index(pair) for pairs in GROUP_PAIRS for pair in pairs]
    x = np.asarray(r_emb_inputs).reshape(CHUNKS, CHUNK, FIELDS, HALVES, P).transpose(2, 0, 4, 3, 1)
    w = np.asarray(L0_rec_weight)[order].reshape(len(PAIRS), HALVES, P, EMBED).transpose(0, 2, 1, 3)
    b = np.asarray(L0_rec_bias)[order].reshape(len(PAIRS), HALVES, P).transpose(2, 0, 1)
    arrays = {"x": np.ascontiguousarray(x), "weight": np.ascontiguousarray(w), "bias": np.ascontiguousarray(b)}

    nc = bacc.Bacc("TRN2", target_bir_lowering=False, num_devices=1)
    args = [nc.dram_tensor(name, a.shape, F32, kind="ExternalInput").ap() for name, a in arrays.items()]
    out = nc.dram_tensor("out", (len(PAIRS), CHUNKS, P, HALVES, CHUNK), F32, kind="ExternalOutput").ap()
    bilinear_interactions(nc, *args, out)
    ran = run_bass_kernel_spmd(nc, [arrays], core_ids=[0])

    got = ran.results[0]["out"]
    result = np.empty((BATCH, len(PAIRS), EMBED), np.float32)
    result.reshape(CHUNKS, CHUNK, len(PAIRS), HALVES, P)[:, :, order] = got.transpose(1, 4, 0, 3, 2)
    return result
```
